# Optimizing a Trainium2 kernel written in Bass

```python
import numpy as np
import jax
import jax.numpy as jnp

def _softmax(x, axis=-1):
    return jax.nn.softmax(x, axis=axis)

def _gelu(x):
    return jax.nn.gelu(x, approximate=True)

def _silu(x):
    return jax.nn.silu(x)

def _sigmoid(x):
    return jax.nn.sigmoid(x)

def _layernorm(x, axis=-1, eps=1e-05):
    m = jnp.mean(x, axis=axis, keepdims=True)
    v = jnp.var(x, axis=axis, keepdims=True)
    return (x - m) / jnp.sqrt(v + eps)

def _scatter_add(tgt, idx, src, axis=0):
    return tgt.at[idx].add(src)

def _segment_sum(src, seg, n):
    return jax.ops.segment_sum(src, seg, n)
kernel_name = 'mk_xattn_ffn_d2_seqx_r4_218cd8'

def setup_inputs(seed: int=0):
    np.random.seed(seed)
    _w = jnp.asarray

    def _rec_inputs():
        import jax
        import jax.numpy as jnp
        _rk = jax.random.key(seed)
        x = -0.0002928 + 1 * jax.random.normal(jax.random.fold_in(_rk, 1), (4, 1024, 256), jnp.float32)
        _lenS = 1024 - jax.random.randint(jax.random.fold_in(_rk, 7), (4,), 0, max(1, 1024 // 4) + 1, jnp.int32)
        _lenS2 = 77 - jax.random.randint(jax.random.fold_in(_rk, 8), (4,), 0, max(1, 77 // 4) + 1, jnp.int32)
        _ctx_1024P = jax.random.normal(jax.random.fold_in(_rk, 11), (4, 16, 256), jnp.float32)
        _ctx_1024c = jax.random.dirichlet(jax.random.fold_in(_rk, 511), 0.3 * jnp.ones((16,), jnp.float32), (4, 77))
        _ctx_1024t = jnp.einsum('bsk,bkd->bsd', _ctx_1024c, _ctx_1024P)
        _ctx_1024t = _ctx_1024t * jax.lax.rsqrt(jnp.mean(jnp.square(_ctx_1024t)) + 1e-12) * 0.953939
        ctx_1024 = -1.39393e-06 + 0.999914 * (_ctx_1024t + 0.3 * jax.random.normal(jax.random.fold_in(_rk, 611), (4, 77, 256), jnp.float32))
        _validS = jnp.arange(1024)[None, :] < _lenS[:, None]
        _validS2 = jnp.arange(77)[None, :] < _lenS2[:, None]
        _causal = jnp.tril(jnp.ones((1024, 1024), dtype=bool))
        mask_SxS2_bk1 = jnp.broadcast_to(_validS2[0:1, :], (1024, 77))
        return (x, ctx_1024, mask_SxS2_bk1)
    x, ctx_1024, mask_SxS2_bk1 = _rec_inputs()

    def _L0_xattn_setup():
        import jax, jax.numpy as jnp
        import numpy as np
        B, S, D, H = (2, 512, 256, 16)
        HD = D // H

        def _split_heads(x):
            b, s, _ = x.shape
            return x.reshape(b, s, H, HD).transpose(0, 2, 1, 3)
        key = jax.random.key(seed)
        ks = jax.random.split(key, 12)
        s = 1.0 / np.sqrt(D)
        inp = {'queries': jax.random.normal(ks[0], (B, S, D), jnp.float32), 'keys': jax.random.normal(ks[1], (B, S, D), jnp.float32), 'values': jax.random.normal(ks[2], (B, S, D), jnp.float32), 'attn_mask': jnp.triu(jnp.ones((S, S), bool), k=1), 'W_q': jax.random.normal(ks[3], (D, D), jnp.float32) * s, 'b_q': jnp.zeros((D,), jnp.float32), 'W_k': jax.random.normal(ks[4], (D, D), jnp.float32) * s, 'b_k': jnp.zeros((D,), jnp.float32), 'W_v': jax.random.normal(ks[5], (D, D), jnp.float32) * s, 'b_v': jnp.zeros((D,), jnp.float32), 'W_o': jax.random.normal(ks[6], (D, D), jnp.float32) * s, 'b_o': jnp.zeros((D,), jnp.float32)}
        return inp
    _L0_xattn_all = _L0_xattn_setup()
    _L0_xattn_in = {k: v for k, v in _L0_xattn_all.items() if k in ('W_q', 'b_q', 'W_k', 'b_k', 'W_v', 'b_v', 'W_o', 'b_o')}
    del _L0_xattn_all

    def _L0_ffn_setup():
        import jax, jax.numpy as jnp
        import numpy as np
        TOP_K = 4
        CAP_FACTOR = 4

        def swiglu(x, w1, w2, w3):
            return jax.nn.silu(x @ w1) * (x @ w3) @ w2
        key = jax.random.key(seed)
        ks = jax.random.split(key, 8)
        B, S, D, H, E = (2, 512, 256, 128, 32)
        Hs = 2 * H
        sd = lambda *sh: 1.0 / np.sqrt(sh[-2])
        x = jax.random.normal(ks[0], (B, S, D), dtype=jnp.float32)
        Wg = jax.random.normal(ks[1], (D, E), dtype=jnp.float32) * (1.0 / np.sqrt(D))
        W1 = jax.random.normal(ks[2], (E, D, H), dtype=jnp.float32) * (1.0 / np.sqrt(D))
        W3 = jax.random.normal(ks[3], (E, D, H), dtype=jnp.float32) * (1.0 / np.sqrt(D))
        W2 = jax.random.normal(ks[4], (E, H, D), dtype=jnp.float32) * (1.0 / np.sqrt(H))
        Ws1 = jax.random.normal(ks[5], (D, Hs), dtype=jnp.float32) * (1.0 / np.sqrt(D))
        Ws3 = jax.random.normal(ks[6], (D, Hs), dtype=jnp.float32) * (1.0 / np.sqrt(D))
        Ws2 = jax.random.normal(ks[7], (Hs, D), dtype=jnp.float32) * (1.0 / np.sqrt(Hs))
        return {'x': x, 'Wg': Wg, 'W1': W1, 'W2': W2, 'W3': W3, 'Ws1': Ws1, 'Ws2': Ws2, 'Ws3': Ws3}
    _L0_ffn_all = _L0_ffn_setup()
    _L0_ffn_in = {k: v for k, v in _L0_ffn_all.items() if k in ('Wg', 'W1', 'W2', 'W3', 'Ws1', 'Ws2', 'Ws3')}
    del _L0_ffn_all

    def _L1_xattn_setup():
        import jax, jax.numpy as jnp
        import numpy as np
        D_MODEL = 256
        N_HEADS = 16
        key = jax.random.key(seed)
        ks = jax.random.split(key, 11)
        B, L, S, D = (2, 512, 512, D_MODEL)
        s = 1.0 / np.sqrt(D)
        return {'Q': jax.random.normal(ks[0], (B, L, D), jnp.float32), 'K': jax.random.normal(ks[1], (B, S, D), jnp.float32), 'V': jax.random.normal(ks[2], (B, S, D), jnp.float32), 'Wq': jax.random.normal(ks[3], (D, D), jnp.float32) * s, 'bq': jnp.zeros((D,), jnp.float32), 'Wk': jax.random.normal(ks[4], (D, D), jnp.float32) * s, 'bk': jnp.zeros((D,), jnp.float32), 'Wv': jax.random.normal(ks[5], (D, D), jnp.float32) * s, 'bv': jnp.zeros((D,), jnp.float32), 'We': jax.random.normal(ks[6], (D, D), jnp.float32) * s, 'be': jnp.zeros((D,), jnp.float32)}
    _L1_xattn_all = _L1_xattn_setup()
    _L1_xattn_in = {k: v for k, v in _L1_xattn_all.items() if k in ('Wq', 'bq', 'Wk', 'bk', 'Wv', 'bv', 'We', 'be')}
    del _L1_xattn_all

    def _L1_ffn_setup():
        import jax, jax.numpy as jnp
        import numpy as np
        import math
        D_IN = 256
        FEATURES = (1024, 1024, 256)
        BATCH, SEQ = (8, 512)

        def _conn_dense(kernel_bool, x):
            w = jnp.where(kernel_bool, jnp.float32(1.0), jnp.float32(-1.0))
            return x @ w
        key = jax.random.key(seed)
        kx, kk0, kk1, kk2 = jax.random.split(key, 4)
        x = jax.random.normal(kx, (BATCH, SEQ, D_IN), dtype=jnp.float32)
        k0 = jax.random.randint(kk0, (2 * D_IN, FEATURES[0]), 0, 2).astype(jnp.bool_)
        k1 = jax.random.randint(kk1, (FEATURES[0], FEATURES[1]), 0, 2).astype(jnp.bool_)
        k2 = jax.random.randint(kk2, (FEATURES[1], FEATURES[2]), 0, 2).astype(jnp.bool_)
        s0 = jnp.asarray(1.0 / math.sqrt(2 * D_IN), dtype=jnp.float32)
        s1 = jnp.asarray(1.0 / math.sqrt(FEATURES[0]), dtype=jnp.float32)
        s2 = jnp.asarray(1.0 / math.sqrt(FEATURES[1]), dtype=jnp.float32)
        return {'x': x, 'k0': k0, 'k1': k1, 'k2': k2, 's0': s0, 's1': s1, 's2': s2}
    _L1_ffn_all = _L1_ffn_setup()
    _L1_ffn_in = {k: v for k, v in _L1_ffn_all.items() if k in ('k0', 'k1', 'k2', 's0', 's1', 's2')}
    del _L1_ffn_all
    return {'x': x, 'ctx_1024': ctx_1024, 'mask_SxS2_bk1': mask_SxS2_bk1, 'L0_xattn_W_q': _L0_xattn_in['W_q'], 'L0_xattn_b_q': _L0_xattn_in['b_q'], 'L0_xattn_W_k': _L0_xattn_in['W_k'], 'L0_xattn_b_k': _L0_xattn_in['b_k'], 'L0_xattn_W_v': _L0_xattn_in['W_v'], 'L0_xattn_b_v': _L0_xattn_in['b_v'], 'L0_xattn_W_o': _L0_xattn_in['W_o'], 'L0_xattn_b_o': _L0_xattn_in['b_o'], 'L0_ffn_Wg': _L0_ffn_in['Wg'], 'L0_ffn_W1': _L0_ffn_in['W1'], 'L0_ffn_W2': _L0_ffn_in['W2'], 'L0_ffn_W3': _L0_ffn_in['W3'], 'L0_ffn_Ws1': _L0_ffn_in['Ws1'], 'L0_ffn_Ws2': _L0_ffn_in['Ws2'], 'L0_ffn_Ws3': _L0_ffn_in['Ws3'], 'L1_xattn_Wq': _L1_xattn_in['Wq'], 'L1_xattn_bq': _L1_xattn_in['bq'], 'L1_xattn_Wk': _L1_xattn_in['Wk'], 'L1_xattn_bk': _L1_xattn_in['bk'], 'L1_xattn_Wv': _L1_xattn_in['Wv'], 'L1_xattn_bv': _L1_xattn_in['bv'], 'L1_xattn_We': _L1_xattn_in['We'], 'L1_xattn_be': _L1_xattn_in['be'], 'L1_ffn_k0': _L1_ffn_in['k0'], 'L1_ffn_k1': _L1_ffn_in['k1'], 'L1_ffn_k2': _L1_ffn_in['k2'], 'L1_ffn_s0': _L1_ffn_in['s0'], 'L1_ffn_s1': _L1_ffn_in['s1'], 'L1_ffn_s2': _L1_ffn_in['s2']}

def reference(x, ctx_1024, mask_SxS2_bk1, L0_xattn_W_q, L0_xattn_b_q, L0_xattn_W_k, L0_xattn_b_k, L0_xattn_W_v, L0_xattn_b_v, L0_xattn_W_o, L0_xattn_b_o, L0_ffn_Wg, L0_ffn_W1, L0_ffn_W2, L0_ffn_W3, L0_ffn_Ws1, L0_ffn_Ws2, L0_ffn_Ws3, L1_xattn_Wq, L1_xattn_bq, L1_xattn_Wk, L1_xattn_bk, L1_xattn_Wv, L1_xattn_bv, L1_xattn_We, L1_xattn_be, L1_ffn_k0, L1_ffn_k1, L1_ffn_k2, L1_ffn_s0, L1_ffn_s1, L1_ffn_s2):
    import jax
    import jax.numpy as jnp

    def _L0_xattn_ref(queries, keys, values, attn_mask, W_q, b_q, W_k, b_k, W_v, b_v, W_o, b_o):
        import jax, jax.numpy as jnp
        import numpy as np
        B, S, D, H = (2, 512, 256, 16)
        HD = D // H

        def _split_heads(x):
            b, s, _ = x.shape
            return x.reshape(b, s, H, HD).transpose(0, 2, 1, 3)
        Q = _split_heads(queries @ W_q + b_q)
        K = _split_heads(keys @ W_k + b_k)
        V = _split_heads(values @ W_v + b_v)
        scale = 1.0 / np.sqrt(HD)
        scores = jnp.einsum('bhqd,bhkd->bhqk', Q, K) * scale
        scores = jnp.where(attn_mask, jnp.float32(-1000000000.0), scores)
        probs = jax.nn.softmax(scores, axis=-1)
        ctx = jnp.einsum('bhqk,bhkd->bhqd', probs, V)
        ctx = ctx.transpose(0, 2, 1, 3).reshape(queries.shape[0], queries.shape[1], D)
        return ctx @ W_o + b_o

    def _L0_ffn_ref(x, Wg, W1, W2, W3, Ws1, Ws2, Ws3):
        import jax, jax.numpy as jnp
        import numpy as np
        TOP_K = 4
        CAP_FACTOR = 4

        def swiglu(x, w1, w2, w3):
            return jax.nn.silu(x @ w1) * (x @ w3) @ w2
        B, S, D = x.shape
        E = Wg.shape[1]
        T = B * S
        xf = x.reshape(T, D)
        scores = jax.nn.softmax(xf @ Wg, axis=-1)
        weights, indices = jax.lax.top_k(scores, TOP_K)
        P = T * TOP_K
        pair_expert = indices.reshape(-1)
        pair_token = jnp.repeat(jnp.arange(T), TOP_K)
        pair_weight = weights.reshape(-1).astype(xf.dtype)
        C = CAP_FACTOR * P // E
        y = jnp.zeros_like(xf)
        for e in range(E):
            pos = jnp.nonzero(pair_expert == e, size=C, fill_value=P)[0]
            valid = pos < P
            safe = jnp.minimum(pos, P - 1)
            tok = jnp.where(valid, pair_token[safe], 0)
            w = jnp.where(valid, pair_weight[safe], 0.0)
            xg = xf[tok]
            out = swiglu(xg, W1[e], W2[e], W3[e]) * w[:, None]
            y = y.at[tok].add(out)
        z = swiglu(xf, Ws1, Ws2, Ws3)
        return (y + z).reshape(B, S, D)

    def _L1_xattn_ref(Q, K, V, Wq, bq, Wk, bk, Wv, bv, We, be):
        import jax, jax.numpy as jnp
        import numpy as np
        D_MODEL = 256
        N_HEADS = 16
        B, L, D = Q.shape
        S = K.shape[1]
        H = N_HEADS
        E = D // H
        q = (Q @ Wq + bq).reshape(B, L, H, E)
        k = (K @ Wk + bk).reshape(B, S, H, E)
        v = (V @ Wv + bv).reshape(B, S, H, E)
        scale = 1.0 / np.sqrt(E)
        scores = jnp.einsum('blhe,bshe->bhls', q, k)
        A = jax.nn.softmax(scale * scores, axis=-1)
        out = jnp.einsum('bhls,bshd->blhd', A, v).reshape(B, L, H * E)
        return out @ We + be

    def _L1_ffn_ref(x, k0, k1, k2, s0, s1, s2):
        import jax, jax.numpy as jnp
        import numpy as np
        import math
        D_IN = 256
        FEATURES = (1024, 1024, 256)
        BATCH, SEQ = (8, 512)

        def _conn_dense(kernel_bool, x):
            w = jnp.where(kernel_bool, jnp.float32(1.0), jnp.float32(-1.0))
            return x @ w
        h = jnp.concatenate([x, -x], axis=-1)
        h = s0 * _conn_dense(k0, h)
        h = jax.nn.relu(h) * 2
        h = s1 * _conn_dense(k1, h)
        h = jax.nn.relu(h) * 2
        h = s2 * _conn_dense(k2, h)
        return h
    x = x + _L0_xattn_ref(_layernorm(x, axis=-1), ctx_1024, ctx_1024, mask_SxS2_bk1, L0_xattn_W_q, L0_xattn_b_q, L0_xattn_W_k, L0_xattn_b_k, L0_xattn_W_v, L0_xattn_b_v, L0_xattn_W_o, L0_xattn_b_o)
    x = x + _L0_ffn_ref(_layernorm(x, axis=-1), L0_ffn_Wg, L0_ffn_W1, L0_ffn_W2, L0_ffn_W3, L0_ffn_Ws1, L0_ffn_Ws2, L0_ffn_Ws3)
    x = x + _L1_xattn_ref(_layernorm(x, axis=-1), ctx_1024, ctx_1024, L1_xattn_Wq, L1_xattn_bq, L1_xattn_Wk, L1_xattn_bk, L1_xattn_Wv, L1_xattn_bv, L1_xattn_We, L1_xattn_be)
    x = x + _L1_ffn_ref(_layernorm(x, axis=-1), L1_ffn_k0, L1_ffn_k1, L1_ffn_k2, L1_ffn_s0, L1_ffn_s1, L1_ffn_s2)
    return x

_drawn_inputs = setup_inputs


def setup_inputs(seed=0):
    import zlib

    import numpy as np

    out = dict(_drawn_inputs(seed))
    spreads = {'L0_xattn_b_q': (0.0, 0.335),
     'L0_xattn_b_k': (0.0, 0.8),
     'L0_xattn_b_v': (0.0, 0.1),
     'L0_xattn_b_o': (0.0, 0.1),
     'L1_xattn_bq': (0.0, 0.537),
     'L1_xattn_bk': (0.0, 0.8),
     'L1_xattn_bv': (0.0, 0.1),
     'L1_xattn_be': (0.0, 0.1)}
    factors = {}
    for name, (base, spread) in spreads.items():
        noise = np.random.default_rng([zlib.crc32(name.encode()), seed]).standard_normal(out[name].shape)
        drawn = base * np.exp(spread * noise) if base else spread * noise
        out[name] = jnp.asarray(drawn.astype(out[name].dtype))
    for name, factor in factors.items():
        out[name] = (out[name] * factor).astype(out[name].dtype)
    return out
```

```python
from contextlib import ExitStack

import concourse.bass as bass
from concourse import mybir

F32, F32R = mybir.dt.float32, mybir.dt.float32r
BF16, F16 = mybir.dt.bfloat16, mybir.dt.float16
I32, U32, U8 = mybir.dt.int32, mybir.dt.uint32, mybir.dt.uint8
ALU = mybir.AluOpType
ACT = mybir.ActivationFunctionType
X_AXIS = mybir.AxisListType.X
ds = bass.ds

P = 128
BATCH, SEQ, D = 4, 1024, 256
KC = D // P
TOKENS = BATCH * SEQ
TILES = TOKENS // P
MT = 4
MACROS = TILES // MT
MW = MT * P
BT = SEQ // P
HEADS, HD = 16, 16
KEYS, KPAD = 77, 80
HH = HEADS // 2
PCH = HEADS * KPAD // P
VW = HD + 1
HEAD0 = [min(c * P // KPAD, HEADS - 3) for c in range(PCH)]
SCALE = 1.0 / 4.0
MASKED = -float(2 ** 60)
EPS = 1e-5
EXPERTS, TOPK, HID = 32, 4, 128
CAP = 4 * TOKENS * TOPK // EXPERTS
SLOTS = EXPERTS * CAP
ETILES = TOKENS * TOPK // P + EXPERTS
AHEAD = 8
SPARE = EXPERTS * P
SHID = 256
FEAT = 1024
FC = FEAT // P


def below(t, k):
    return isinstance(t, int) and t < k


def every(eng, n, body, width=2):
    for u in range(width):
        body(u, u, 0)
    with eng.Fori(1, n // width - 1) as g:
        for u in range(width):
            body(g * width + u, u, g)
    for u in range(width):
        body(n - width + u, u, n // width - 1)


def from_end(t, n, k):
    return isinstance(t, int) and t >= n - k


class Steps:

    def __init__(self, eng, sem, per=0):
        self.eng, self.sem, self.per, self.base, self.n = eng, sem, per, 0, 0

    def tile(self, t):
        assert not self.n or self.n == self.per, (self.n, self.per)
        self.base, self.n = t * self.per, 0

    def done(self, ins):
        self.n += 1
        ins.then_inc(self.sem, 1)
        self.eng.wait_ge(self.sem, self.base + self.n)


def build(nc, a, out):
    whole = ExitStack()
    n_sem = [0]

    in_use = []

    def sem(name):
        n_sem[0] += 1
        in_use.append(nc.alloc_semaphore(f"{name}_{n_sem[0]}"))
        return in_use[-1]

    def retire():
        nc.clear_and_free_semaphores(in_use)
        nc.all_engine_barrier()
        in_use.clear()

    def space(stack, name, shape, dt=F32):
        n_sem[0] += 1
        return stack.enter_context(nc.sbuf_tensor(f"{name}_{n_sem[0]}", shape, dt))

    def banks(stack, name, shape, dt=F32):
        n_sem[0] += 1
        return stack.enter_context(nc.psum_tensor(f"{name}_{n_sem[0]}", shape, dt))

    def always(name, shape, dt=F32):
        return space(whole, name, shape, dt)

    v_rows = nc.dram_tensor("v_rows", (BATCH, HEADS, KPAD, VW), F32, kind="Internal").ap()
    xn_rows = nc.dram_tensor("xn_rows", (TOKENS, D), F32, kind="Internal").ap()
    token_of = nc.dram_tensor("token_of", (SLOTS + SPARE, 1), I32, kind="Internal").ap()
    y_rows = nc.dram_tensor("y_rows", (ETILES * P, D), F32, kind="Internal").ap()
    plan_rows = nc.dram_tensor("plan_rows", (2, 2 * P), I32, kind="Internal").ap()

    X = always("X", [P, TILES, D])
    ident = always("ident", [P, P])
    ident_b = always("ident_b", [P, P], BF16)
    ident_h = always("ident_h", [P, P], F16)
    ones = always("ones", [P, P])
    ones_b = always("ones_b", [P, P], BF16)
    before = always("before", [P, P], BF16)
    head_of_row = always("head_of_row", [P, HH])
    head_of_pair = always("head_of_pair", [P, PCH, HEADS])
    expert_id = always("expert_id", [P, EXPERTS])
    token_id = always("token_id", [P, TILES], I32)
    tile_id = always("tile_id", [P, 2])
    minus_half = always("minus_half", [P, MT])
    ctxT = always("ctxT", [P, KC, BATCH * KEYS])
    slots = always("slots", [P, TILES * TOPK], I32)
    gates = always("gates", [P, TILES * TOPK])
    mask8 = always("mask8", [P, SEQ // P, KEYS], BF16)

    def setup():
        st = ExitStack()
        ctx = space(st, "ctx", [KEYS, BATCH, D])
        mask_u = space(st, "mask_u", [P, SEQ // P, KEYS], U8)
        iota_i = space(st, "iota_i", [P, EXPERTS + 2], I32)
        zero_i = space(st, "zero_i", [P, (SLOTS + SPARE) // P], I32)
        zero_v = space(st, "zero_v", [BATCH * HEADS, (KPAD - KEYS) * VW])
        ps = banks(st, "ps", [P, 2, BATCH, P])
        x_in, ctx_in, mask_in, cleared = sem("x_in"), sem("ctx_in"), sem("mask_in"), sem("cleared")
        consts, ident_ready, ctx_turned, ctx_out, zeroed = (
            sem("consts"), sem("ident_ready"), sem("ctx_turned"), sem("ctx_out"), sem("zeroed"))
        dve_own = sem("dve_own")
        with nc.Block() as block:

            @block.sync
            def _(sp):
                sp.dma_start(ctx[:], a["ctx"].rearrange("b k d -> k b d")).then_inc(ctx_in, 16)
                sp.dma_start(mask_u[:], a["mask"].rearrange("(n p) k -> p n k", p=P)).then_inc(mask_in, 16)
                sp.dma_start(X[:], a["x"].rearrange("b (n p) d -> p (b n) d", p=P)).then_inc(x_in, 16)
                sp.wait_ge(zeroed, 2)
                sp.dma_start(token_of.rearrange("(p n) one -> p (n one)", p=P), zero_i[:]).then_inc(cleared, 16)
                sp.dma_start(v_rows[:, :, KEYS:KPAD, :].rearrange("b h k v -> (b h) (k v)"),
                             zero_v[:]).then_inc(cleared, 16)
                sp.wait_ge(cleared, 32)
                sp.wait_ge(x_in, 16)

            @block.gpsimd
            def _(pool):
                own = Steps(pool, consts)
                pool.memset(ones[:], 1.0)
                pool.memset(minus_half[:], -0.5)
                pool.memset(zero_i[:], 0).then_inc(zeroed, 1)
                pool.memset(zero_v[:], 0.0).then_inc(zeroed, 1)
                pool.memset(head_of_pair[:], 1.0)
                own.done(pool.memset(ones_b[:], 1.0))
                pool.affine_select(out=ident[:], in_=ones[:], compare_op=ALU.is_equal, fill=0.0, base=0,
                                   pattern=[[-1, P]], channel_multiplier=1).then_inc(ident_ready, 1)
                pool.affine_select(out=ident_b[:], in_=ones[:], compare_op=ALU.is_equal, fill=0.0, base=0,
                                   pattern=[[-1, P]], channel_multiplier=1)
                pool.affine_select(out=ident_h[:], in_=ones[:], compare_op=ALU.is_equal, fill=0.0, base=0,
                                   pattern=[[-1, P]], channel_multiplier=1)
                pool.affine_select(out=before[:], in_=ones[:], compare_op=ALU.is_gt, fill=0.0, base=0,
                                   pattern=[[1, P]], channel_multiplier=-1)
                own.done(pool.affine_select(out=head_of_row[:], in_=ones[:, 0:HH], compare_op=ALU.is_ge,
                                            fill=0.0, base=0, pattern=[[-HD, HH]], channel_multiplier=1))
                pool.affine_select(out=head_of_row[:], in_=head_of_row[:], compare_op=ALU.is_ge,
                                   fill=0.0, base=HD - 1, pattern=[[HD, HH]], channel_multiplier=-1)
                own.done(pool.affine_select(out=head_of_pair[:], in_=head_of_pair[:], compare_op=ALU.is_ge,
                                            fill=0.0, base=0, pattern=[[P, PCH], [-KPAD, HEADS]],
                                            channel_multiplier=1))
                pool.affine_select(out=head_of_pair[:], in_=head_of_pair[:], compare_op=ALU.is_ge, fill=0.0,
                                   base=KPAD - 1, pattern=[[-P, PCH], [KPAD, HEADS]], channel_multiplier=-1)
                pool.iota(token_id[:], pattern=[[P, TILES]], base=0, channel_multiplier=1)
                pool.iota(iota_i[:, 0:EXPERTS], pattern=[[1, EXPERTS]], base=0, channel_multiplier=0)
                own.done(pool.iota(iota_i[:, EXPERTS:], pattern=[[P, 2]], base=0, channel_multiplier=1))

            @block.vector
            def _(dve):
                own = Steps(dve, dve_own)
                dve.wait_ge(mask_in, 16)
                dve.tensor_scalar(mask8[:], mask_u[:], MASKED, None, ALU.mult)
                dve.wait_ge(consts, 4)
                dve.tensor_copy(expert_id[:], iota_i[:, 0:EXPERTS])
                dve.tensor_copy(tile_id[:], iota_i[:, EXPERTS:])
                for c in range(KC):
                    dve.wait_ge(ctx_turned, c + 1)
                    dve.tensor_copy(ctxT[:, c, :].rearrange("p (b k) -> p b k", k=KEYS), ps[:, c, :, 0:KEYS])

            @block.tensor
            def _(pe):
                pe.wait_ge(ident_ready, 1)
                pe.wait_ge(ctx_in, 16)
                for c in range(KC):
                    for b in range(BATCH):
                        last = pe.transpose(ps[:, c, b, 0:KEYS], ctx[:, b, c * P:(c + 1) * P], ident[0:KEYS, 0:KEYS])
                    last.then_inc(ctx_turned, 1)
        st.close()

    def keys_values(w, KB, V1, V2, V3, binary_out):
        st = ExitStack()
        wk = space(st, "wk", [P, KC, D])
        wv = space(st, "wv", [P, KC, D])
        bk = space(st, "bk", [P, KC])
        bv = space(st, "bv", [1, D])
        KT = space(st, "KT", [P, KC, BATCH, KEYS])
        VS = space(st, "VS", [KEYS, BATCH, HEADS, VW])
        VR = space(st, "VR", [P, BATCH, PCH, VW])
        VC = space(st, "VC", [P, BATCH, PCH, 3, VW])
        psK = banks(st, "psK", [P, KC, 512])
        psV = banks(st, "psV", [P, BATCH, 512])
        loaded, k_done, k_out, v_done, v_out, v_stored, v_back = (sem(s) for s in (
            "loaded", "k_done", "k_out", "v_done", "v_out", "v_stored", "v_back"))
        own_s = sem("own")
        binary = BinaryWeights(st, *binary_out) if binary_out else None
        with nc.Block() as block:

            @block.sync
            def _(sp):
                sp.dma_start(wk[:], w["wk"].rearrange("(c p) n -> p c n", p=P)).then_inc(loaded, 16)
                sp.dma_start(wv[:], w["wv"].rearrange("(c p) n -> p c n", p=P)).then_inc(loaded, 16)
                with nc.allow_non_contiguous_dma("a bias, one value a partition"):
                    sp.dma_start(bk[:], w["bk"].rearrange("(c p) -> p c", p=P)).then_inc(loaded, 16)
                sp.dma_start(bv[:], w["bv"].rearrange("(o n) -> o n", o=1)).then_inc(loaded, 16)
                if binary:
                    binary.load(sp)
                for b in range(BATCH):
                    sp.wait_ge(v_out, b + 1)
                    sp.dma_start(v_rows[b, :, 0:KEYS, :].rearrange("h k v -> k h v"), VS[:, b]).then_inc(v_stored, 16)
                sp.wait_ge(v_stored, 16 * BATCH)
                for b in range(BATCH):
                    sp.dma_start(VR[:, b], v_rows[b].rearrange("h k v -> (h k) v").rearrange(
                        "(c p) v -> p c v", p=P)).then_inc(v_back, 16)

            @block.tensor
            def _(pe):
                pe.wait_ge(loaded, 64)
                for b in range(BATCH):
                    for c in range(KC):
                        pe.matmul(psV[0:KEYS, b, 0:D], ctxT[:, c, b * KEYS:(b + 1) * KEYS], wv[:, c, :],
                                  start=c == 0, stop=False)
                    pe.matmul(psV[0:KEYS, b, 0:D], ones[0:1, 0:KEYS], bv[:, :], start=False,
                              stop=True).then_inc(v_done, 1)
                for o in range(KC):
                    for c in range(KC):
                        last = pe.matmul(psK[:, o, 0:BATCH * KEYS], wk[:, c, o * P:(o + 1) * P], ctxT[:, c, :],
                                         start=c == 0, stop=c == KC - 1)
                    last.then_inc(k_done, 1)

            @block.scalar
            def _(act):
                for o in range(KC):
                    act.wait_ge(k_done, o + 1)
                    act.activation(KT[:, o], psK[:, o, 0:BATCH * KEYS].rearrange("p (b k) -> p b k", k=KEYS),
                                   ACT.Identity, bias=bk[:, o:o + 1]).then_inc(k_out, 1)

            @block.vector
            def _(dve):
                own = Steps(dve, own_s)
                own.done(dve.memset(VS[:], 1.0))
                for b in range(BATCH):
                    dve.wait_ge(v_done, b + 1)
                    dve.tensor_copy(VS[:, b, :, 0:HD], psV[0:KEYS, b, 0:D].rearrange(
                        "p (h v) -> p h v", v=HD)).then_inc(v_out, 1)
                if binary:
                    binary.prepare(dve)
                for o in range(KC):
                    dve.wait_ge(k_out, o + 1)
                    for b in range(BATCH):
                        dve.tensor_tensor(
                            KB[:, b, o], KT[:, o, b].unsqueeze(1).to_broadcast([P, HH, KEYS]),
                            head_of_row[:].unsqueeze(2).to_broadcast([P, HH, KEYS]), ALU.mult)
                dve.wait_ge(v_back, 16 * BATCH)
                for c in range(PCH):
                    last = dve.tensor_tensor(
                        VC[:, :, c], VR[:, :, c].unsqueeze(2).to_broadcast([P, BATCH, 3, VW]),
                        head_of_pair[:, c, HEAD0[c]:HEAD0[c] + 3].unsqueeze(1).unsqueeze(3).to_broadcast(
                            [P, BATCH, 3, VW]), ALU.mult)
                own.done(last)
                v = VC[:].rearrange("p b c j v -> p (b c j v)")
                own.done(dve.tensor_copy(V1[:].rearrange("p b c v -> p (b c v)"), v))
                own.done(dve.tensor_tensor(v, v, V1[:].rearrange("p b c v -> p (b c v)"), ALU.subtract))
                own.done(dve.tensor_copy(V2[:].rearrange("p b c v -> p (b c v)"), v))
                dve.tensor_tensor(V3[:].rearrange("p b c v -> p (b c v)"), v,
                                  V2[:].rearrange("p b c v -> p (b c v)"), ALU.subtract)
        st.close()

    class Norm:

        def __init__(self, st):
            self.st6 = space(st, "st6", [P, MT, 6])
            self.mv = [space(st, "mv", [P, MT, 2]) for _ in range(2)]
            self.rstd = [space(st, "rstd", [P, MT]) for _ in range(2)]
            self.var = [space(st, "var", [P, MT]) for _ in range(2)]
            self.summed, self.var_ready, self.var_eps, self.rstd_ready, self.held = (
                sem(n) for n in ("stats_summed", "var_ready", "var_eps", "rstd_ready", "held"))

        def stats(self, dve, m, u):
            for t in range(MT):
                last = dve.bn_stats(self.st6[:, t, :], X[:, ds(m * MT + t, 1), :])
            last.then_inc(self.summed, 1)
            dve.wait_ge(self.summed, m + 1)
            dve.sem_inc(self.held, 1)
            for t in range(MT):
                last = dve.bn_aggr(self.mv[u][:, t, :], self.st6[:, t, :])
            last.then_inc(self.var_ready, 1)

        def power(self, pool, m, u):
            pool.wait_ge(self.var_ready, m + 1)
            pool.sem_inc(self.held, 1)
            pool.tensor_scalar(self.var[u][:], self.mv[u][:, :, 1], EPS, None, ALU.add).then_inc(self.var_eps, 1)
            pool.wait_ge(self.var_eps, m + 1)
            pool.tensor_tensor(self.rstd[u][:], self.var[u][:], minus_half[:], ALU.pow).then_inc(self.rstd_ready, 1)

        def apply(self, dve, m, u, XN, ready):
            dve.wait_ge(self.rstd_ready, m + 1)
            for t in range(MT):
                last = dve.tensor_scalar(XN[:, t:t + 1, :], X[:, ds(m * MT + t, 1), :], self.mv[u][:, t, 0:1],
                                         self.rstd[u][:, t:t + 1], ALU.subtract, ALU.mult)
            last.then_inc(ready, 1)

    def turn(pe, XN, psX):
        for c in range(KC):
            for t in range(MT):
                last = pe.transpose(psX[:, c, t * P:(t + 1) * P], XN[:, t, c * P:(c + 1) * P], ident[:])
        return last

    def queries(w, QT, after_experts):
        st = ExitStack()
        XN = [space(st, "XN", [P, MT, D]) for _ in range(2)]
        XH = [space(st, "XH", [P, KC, MW], F32R) for _ in range(2)]
        XL = [space(st, "XL", [P, KC, MW], F32R) for _ in range(2)]
        wq = space(st, "wq", [P, KC, D])
        WH = space(st, "WH", [P, KC, D], F32R)
        WL = space(st, "WL", [P, KC, D], F32R)
        bq = space(st, "bq", [P, KC])
        norm = Norm(st)
        combine = Combine(st) if after_experts else None
        psX = [banks(st, "psX", [P, KC, MW]) for _ in range(2)]
        psQ = banks(st, "psQ", [P, KC, MW])
        loaded, w_hi, w_lo, xn_ready, turned, x_hi, x_lo, q_done, q_out = (sem(s) for s in (
            "loaded", "w_hi", "w_lo", "xn_ready", "turned", "x_hi", "x_lo", "q_done", "q_out"))
        with nc.Block() as block:

            @block.sync
            def _(sp):
                sp.dma_start(wq[:], w["wq"].rearrange("(c p) n -> p c n", p=P)).then_inc(loaded, 16)
                with nc.allow_non_contiguous_dma("a bias, one value a partition"):
                    sp.dma_start(bq[:], w["bq"].rearrange("(c p) -> p c", p=P)).then_inc(loaded, 16)

            @block.gpsimd
            def _(pool):
                if not combine:
                    every(pool, MACROS, lambda m, u, g: norm.power(pool, m, u))
                    return
                combine.clear(pool)
                combine.gather(pool, 0, 0)

                def body(m, u, g):
                    if not from_end(m, MACROS, 1):
                        combine.gather(pool, m + 1, 1 - u)
                    norm.power(pool, m, u)
                every(pool, MACROS, body)

            @block.vector
            def _(dve):
                def turned_in(m, u):
                    if not below(m, 2):
                        dve.wait_ge(turned, m - 1)
                    norm.apply(dve, m, u, XN[u], xn_ready)

                def low(m, u):
                    dve.wait_ge(x_hi, m + 1)
                    if not below(m, 2):
                        dve.wait_ge(q_done, m * KC - KC)
                    dve.tensor_tensor(XL[u][:], psX[u][:], XH[u][:], ALU.subtract).then_inc(x_lo, 1)

                def split_weights():
                    dve.wait_ge(w_hi, 1)
                    dve.tensor_tensor(WL[:], wq[:], WH[:], ALU.subtract).then_inc(w_lo, 1)

                if combine:
                    split_weights()

                    def summed(m, u, g):
                        combine.add(dve, m)
                        norm.stats(dve, m, u)
                        if not below(m, 1):
                            turned_in(m - 1, 1 - u)
                            low(m - 1, 1 - u)
                    every(dve, MACROS, summed)
                    turned_in(MACROS - 1, 1)
                    low(MACROS - 1, 1)
                    return
                norm.stats(dve, 0, 0)
                turned_in(0, 0)
                norm.stats(dve, 1, 1)
                split_weights()

                def body(m, u, g):
                    if not from_end(m, MACROS, 1):
                        turned_in(m + 1, 1 - u)
                    if not from_end(m, MACROS, 2):
                        norm.stats(dve, m + 2, u)
                    low(m, u)
                every(dve, MACROS, body)

            @block.scalar
            def _(act):
                act.wait_ge(loaded, 32)
                act.activation(WH[:], wq[:], ACT.Copy).then_inc(w_hi, 1)

                def high(m, u):
                    act.wait_ge(turned, m + 1)
                    if not below(m, 2):
                        act.wait_ge(q_done, (m - 1) * KC)
                    act.activation(XH[u][:], psX[u][:], ACT.Copy).then_inc(x_hi, 1)
                high(0, 0)

                def body(m, u, g):
                    if not (isinstance(m, int) and m == MACROS - 1):
                        high(m + 1, 1 - u)
                    for o in range(KC):
                        act.wait_ge(q_done, m * KC + o + 1)
                        act.activation(QT[:, o, ds(m * MW, MW)], psQ[:, o], ACT.Identity,
                                       bias=bq[:, o:o + 1]).then_inc(q_out, 1)
                every(act, MACROS, body)

            @block.tensor
            def _(pe):
                pe.wait_ge(xn_ready, 1)
                turn(pe, XN[0], psX[0]).then_inc(turned, 1)
                pe.wait_ge(w_lo, 1)

                def body(m, u, g):
                    if not (isinstance(m, int) and m == MACROS - 1):
                        pe.wait_ge(xn_ready, m + 2)
                        if not below(m, 1):
                            pe.wait_ge(x_lo, m)
                        turn(pe, XN[1 - u], psX[1 - u]).then_inc(turned, 1)
                    pe.wait_ge(x_lo, m + 1)
                    for o in range(KC):
                        if not below(m, 1):
                            pe.wait_ge(q_out, (m - 1) * KC + o + 1)
                        terms = [(W, XX, c) for c in range(KC) for W, XX in ((WH, XH), (WH, XL), (WL, XH))]
                        for n, (W, XX, c) in enumerate(terms):
                            last = pe.matmul(psQ[:, o], W[:, c, o * P:(o + 1) * P], XX[u][:, c],
                                             start=n == 0, stop=n == len(terms) - 1)
                        last.then_inc(q_done, 1)
                every(pe, MACROS, body)
        st.close()

    def attend(w, QT, KB, V1, V2, V3, masked):
        st = ExitStack()
        QS = [space(st, "QS", [P, KC, P]) for _ in range(2)]
        DF = [space(st, "DF", [P, HEADS, KEYS]) for _ in range(2)]
        PR = [space(st, "PR", [P, HEADS, KEYS]) for _ in range(2)]
        PH = [space(st, "PH", [P, HEADS, KPAD], F16) for _ in range(2)]
        PL = [space(st, "PL", [P, HEADS, KPAD], F16) for _ in range(2)]
        PHT = space(st, "PHT", [P, PCH, P], F16)
        PLT = space(st, "PLT", [P, PCH, P], F16)
        mx = [space(st, "mx", [P, HEADS]) for _ in range(2)]
        rden = space(st, "rden", [P, HEADS])
        CX = [space(st, "CX", [P, HEADS, HD]) for _ in range(2)]
        CT = space(st, "CT", [P, KC, P])
        wo = space(st, "wo", [P, KC, D])
        bo = space(st, "bo", [P, D])
        psS = banks(st, "psS", [P, 2, 2, 512])
        psT = [banks(st, "psT", [P, 1024], F16) for _ in range(2)]
        psO = banks(st, "psO", [P, 512])
        psM = banks(st, "psM", [P, 512])
        loaded, padded, q_staged, scored, shifted, expd, hi_ready, lo_ready = (sem(s) for s in (
            "loaded", "padded", "q_staged", "scored", "shifted", "expd", "hi_ready", "lo_ready"))
        hi_turned, lo_turned, hi_out, lo_out, pv_done, normed, c_turned, c_out, y_done, added, biased = (
            sem(s) for s in ("hi_turned", "lo_turned", "hi_out", "lo_out", "pv_done", "normed", "c_turned",
                             "c_out", "y_done", "added", "biased"))
        max_ready, rden_ready = sem("max_ready"), sem("rden_ready")
        HC = PCH // 2
        with nc.Block() as block:

            @block.sync
            def _(sp):
                sp.dma_start(wo[:], w["wo"].rearrange("(c p) n -> p c n", p=P)).then_inc(loaded, 16)
                sp.dma_start(bo[:], w["bo"].rearrange("(o n) -> o n", o=1).to_broadcast([P, D])).then_inc(loaded, 16)

            @block.gpsimd
            def _(pool):
                for u in range(2):
                    pool.memset(PH[u][:], 0.0).then_inc(padded, 1)
                    pool.memset(PL[u][:], 0.0).then_inc(padded, 1)
                pool.wait_ge(padded, 4)
                pool.wait_ge(loaded, 32)

                def stage(t, u):
                    if not below(t, 2):
                        pool.wait_ge(scored, 2 * (t - 1))
                    pool.tensor_copy(QS[u][:], QT[:, :, ds(t * P, P)]).then_inc(q_staged, 1)
                stage(0, 0)

                def body(t, u, g):
                    if not from_end(t, TILES, 1):
                        stage(t + 1, 1 - u)
                    pool.tensor_tensor(X[:, ds(t, 1), :], X[:, ds(t, 1), :], bo[:].unsqueeze(1),
                                       ALU.add).then_inc(biased, 1)
                    pool.wait_ge(hi_ready, t + 1)
                    if not below(t, 2):
                        pool.wait_ge(lo_turned, 2 * (t - 1))
                    pool.tensor_tensor(PL[u][:, :, 0:KEYS], PR[u][:], PH[u][:, :, 0:KEYS],
                                       ALU.subtract).then_inc(lo_ready, 1)
                every(pool, TILES, body)

            @block.vector
            def _(dve):
                def shift(t, u):
                    for h in range(2):
                        dve.wait_ge(scored, 2 * t + h + 1)
                        s = psS[:, h, :, 0:HH // 2 * KEYS].rearrange("p b (h k) -> p b h k", k=KEYS)
                        m = mx[u][:, h * HH:(h + 1) * HH].rearrange("p (b h) -> p b h", b=2)
                        dve.tensor_reduce(m, s, X_AXIS, ALU.max).then_inc(max_ready, 1)
                        dve.wait_ge(max_ready, 2 * t + h + 1)
                        if not below(t, 2):
                            dve.wait_ge(expd, 2 * (t - 2) + h + 1)
                        dve.tensor_tensor(
                            DF[u][:, h * HH:(h + 1) * HH].rearrange("p (b h) k -> p b h k", b=2), s,
                            m.unsqueeze(3).to_broadcast([P, 2, HH // 2, KEYS]), ALU.subtract).then_inc(shifted, 1)

                shift(0, 0)

                def body(t, u, g):
                    if not from_end(t, TILES, 1):
                        shift(t + 1, 1 - u)
                    for h in range(2):
                        dve.wait_ge(lo_turned, 2 * t + h + 1)
                        if h == 0 and not below(t, 1):
                            dve.wait_ge(pv_done, t)
                        dve.tensor_copy(PLT[:, h * HC:(h + 1) * HC], psT[h][:, 0:HC * P].rearrange(
                            "p (c q) -> p c q", q=P)).then_inc(lo_out, 1)
                    dve.wait_ge(pv_done, t + 1)
                    o = psO[:, 0:HEADS * VW].rearrange("p (h v) -> p h v", v=VW)
                    dve.reciprocal(rden[:], o[:, :, HD]).then_inc(rden_ready, 1)
                    dve.wait_ge(rden_ready, t + 1)
                    if not below(t, 2):
                        dve.wait_ge(c_turned, t - 1)
                    dve.tensor_tensor(CX[u][:], o[:, :, 0:HD], rden[:].unsqueeze(2).to_broadcast([P, HEADS, HD]),
                                      ALU.mult).then_inc(normed, 1)
                    if not below(t, 1):
                        residual(t - 1)

                def residual(t):
                    dve.wait_ge(y_done, t + 1)
                    dve.wait_ge(biased, t + 1)
                    dve.tensor_tensor(X[:, ds(t, 1), :], X[:, ds(t, 1), :], psM[:, D:2 * D].unsqueeze(1),
                                      ALU.add).then_inc(added, 1)
                every(dve, TILES, body)
                residual(TILES - 1)

            @block.scalar
            def _(act):
                act.wait_ge(padded, 4)

                def exps(t, u):
                    for h in range(2):
                        act.wait_ge(shifted, 2 * t + h + 1)
                        if not below(t, 2):
                            act.wait_ge(lo_ready, t - 1)
                        act.activation(PR[u][:, h * HH:(h + 1) * HH], DF[u][:, h * HH:(h + 1) * HH], ACT.Exp,
                                       scale=SCALE).then_inc(expd, 1)
                    act.wait_ge(expd, 2 * t + 2)
                    if not below(t, 2):
                        act.wait_ge(hi_turned, 2 * (t - 1))
                    act.activation(PH[u][:, :, 0:KEYS], PR[u][:], ACT.Copy).then_inc(hi_ready, 1)

                def context_out(t):
                    act.wait_ge(c_turned, t + 1)
                    act.activation(CT[:], psM[:, 0:D].rearrange("p (c q) -> p c q", q=P), ACT.Copy).then_inc(c_out, 1)
                exps(0, 0)

                def body(t, u, g):
                    if not below(t, 1):
                        context_out(t - 1)
                    for h in range(2):
                        act.wait_ge(hi_turned, 2 * t + h + 1)
                        if h == 0 and not below(t, 1):
                            act.wait_ge(pv_done, t)
                        act.activation(PHT[:, h * HC:(h + 1) * HC], psT[h][:, 0:HC * P].rearrange(
                            "p (c q) -> p c q", q=P), ACT.Copy).then_inc(hi_out, 1)
                    if not from_end(t, TILES, 1):
                        exps(t + 1, 1 - u)
                every(act, TILES, body)
                context_out(TILES - 1)

            @block.tensor
            def _(pe):
                def scores(t, u, b):
                    pe.wait_ge(q_staged, t + 1)
                    for h in range(2):
                        if not below(t, 1):
                            pe.wait_ge(shifted, 2 * (t - 1) + h + 1)
                        for k in range(2):
                            s = psS[:, h, k, 0:HH // 2 * KEYS]
                            if masked:
                                pe.matmul(s.rearrange("p (h k) -> p h k", k=KEYS), ident_b[:],
                                          mask8[:, ds(t - b * BT, 1), :].to_broadcast([P, HH // 2, KEYS]),
                                          start=True, stop=False)
                            last = pe.matmul(s, QS[u][:, h, :], KB[:, b, h, k * (HH // 2):(k + 1) * (HH // 2), :],
                                             start=not masked, stop=True)
                        last.then_inc(scored, 1)

                def turn_context(t, u):
                    pe.wait_ge(normed, t + 1)
                    if not below(t, 1):
                        pe.wait_ge(added, t)
                    for c in range(KC):
                        last = pe.transpose(psM[:, c * P:(c + 1) * P],
                                            CX[u][:].rearrange("p h v -> p (h v)")[:, c * P:(c + 1) * P], ident[:])
                    last.then_inc(c_turned, 1)

                def project(t):
                    pe.wait_ge(c_out, t + 1)
                    for c in range(KC):
                        last = pe.matmul(psM[:, D:2 * D], CT[:, c], wo[:, c, :], start=c == 0, stop=c == KC - 1)
                    last.then_inc(y_done, 1)

                def turn_probs(t, part, ready, turned, free):
                    for h in range(2):
                        pe.wait_ge(ready, t + 1)
                        if free is not None:
                            pe.wait_ge(free[0], free[1] + h + 1)
                        for c in range(HC):
                            last = pe.transpose(psT[h][:, c * P:(c + 1) * P],
                                                part[:].rearrange("p h k -> p (h k)")[:, (h * HC + c) * P:
                                                                                      (h * HC + c + 1) * P], ident_h[:])
                        last.then_inc(turned, 1)

                def values(t, b):
                    if not below(t, 1):
                        pe.wait_ge(normed, t)
                    pe.wait_ge(hi_out, 2 * t + 2)
                    pe.wait_ge(lo_out, 2 * t + 2)
                    for c in range(PCH):
                        for part, vs in ((PHT, (V1, V2, V3)), (PLT, (V1, V2))):
                            for v in vs:
                                last = pe.matmul(
                                    psO[:, HEAD0[c] * VW:(HEAD0[c] + 3) * VW], part[:, c], v[:, b, c, :],
                                    start=c == 0 and part is PHT and v is V1,
                                    stop=c == PCH - 1 and part is PLT and v is V2, skip_group_check=True)
                    last.then_inc(pv_done, 1)

                pe.wait_ge(loaded, 32)
                scores(0, 0, 0)

                def body(t, u, b, next_b):
                    if not from_end(t, TILES, 1):
                        scores(t + 1, 1 - u, next_b)
                    if not below(t, 1):
                        turn_context(t - 1, 1 - u)
                    turn_probs(t, PH[u], hi_ready, hi_turned, None if below(t, 1) else (lo_out, 2 * (t - 1)))
                    turn_probs(t, PL[u], lo_ready, lo_turned, (hi_out, 2 * t))
                    if not below(t, 1):
                        project(t - 1)
                    values(t, b)

                for b in range(BATCH):
                    for u in range(2):
                        body(b * BT + u, u, b, b)
                    with pe.Fori(1, BT // 2 - 1) as g:
                        for u in range(2):
                            body(g * 2 + (b * BT + u), u, b, b)
                    for u in range(2):
                        body(b * BT + BT - 2 + u, u, b, b if u == 0 else b + 1)
                turn_context(TILES - 1, 1)
                project(TILES - 1)
        st.close()

    def route(counts, shift):
        st = ExitStack()
        XN = [space(st, "XN", [P, MT, D]) for _ in range(2)]
        XH = space(st, "XH", [P, KC, MW], F32R)
        XL = space(st, "XL", [P, KC, MW], F32R)
        wg = space(st, "wg", [P, KC, P])
        w1 = space(st, "w1", [P, KC, SHID])
        w3 = space(st, "w3", [P, KC, SHID])
        w2 = space(st, "w2", [P, KC, D])
        split = {n: [space(st, n, [P, KC, s[:].shape[2]], F32R) for _ in range(2)] for n, s in
                 (("wg", wg), ("w1", w1), ("w3", w3))}
        norm = Norm(st)
        LT = space(st, "LT", [P, MW])
        SG = space(st, "SG", [P, KC, MW])
        HS = space(st, "HS", [P, KC, MW])
        mx, sm, rs = (space(st, n, [P, MT]) for n in ("mx", "sm", "rs"))
        dl, el, sc, pos, pen = (space(st, n, [P, MT, EXPERTS]) for n in ("dl", "el", "sc", "pos", "pen"))
        top = space(st, "top", [P, MT, 8])
        idx = space(st, "idx", [P, MT, 8], U32)
        idf = space(st, "idf", [P, MT, TOPK])
        hot = space(st, "hot", [P, MT, TOPK, EXPERTS])
        prod = space(st, "prod", [P, MT, TOPK, EXPERTS])
        slotf = space(st, "slotf", [P, MT, TOPK])
        chosen = space(st, "chosen", [P, MT, EXPERTS], BF16)
        slot_s = [space(st, "slot_s", [P, MT * TOPK], I32) for _ in range(2)]
        tok_s = [space(st, "tok_s", [P, MT], I32) for _ in range(2)]
        nt_i = [space(st, "nt_i", [P, EXPERTS], I32) for _ in range(2)]
        ends = [space(st, "ends", [P, EXPERTS]) for _ in range(2)]
        ntile = space(st, "ntile", [P, EXPERTS])
        le, lew = (space(st, n, [P, 2, EXPERTS]) for n in ("le", "lew"))
        ej, sj, aj = (space(st, n, [P, 2]) for n in ("ej", "sj", "aj"))
        plan = space(st, "plan", [P, 2, 2], I32)
        e_i = space(st, "e_i", [P, TILES * TOPK], I32)
        e_f = space(st, "e_f", [P, TILES * TOPK])
        pick = space(st, "pick", [P, TILES * TOPK, EXPERTS])
        psX = banks(st, "psX", [P, KC, MW])
        psH = [banks(st, "psH", [P, MW]) for _ in range(3)]
        psG = banks(st, "psG", [P, MW])
        psR = banks(st, "psR", [P, 512])
        psZ = [banks(st, "psZ", [P, 2, D])[:], psG[:].rearrange("p (t d) -> p t d", d=D)]
        psL = psR[:, 0:MT * EXPERTS].rearrange("p (t e) -> p t e", e=EXPERTS)
        psC = psR[:, MT * EXPERTS:(2 * MT + 1) * EXPERTS].rearrange("p (t e) -> p t e", e=EXPERTS)
        xn_ready, turned, x_hi, x_lo, g_done, g_out, l_done, l_shift, l_exp, chosen_s, c_done, slots_s = (
            sem(s) for s in ("xn_ready", "turned", "x_hi", "x_lo", "g_done", "g_out", "l_done", "l_shift", "l_exp",
                             "chosen", "c_done", "slots_ready"))
        h_done, silu_s, hs_s, z_done, z_added, loaded, w_hi, w_lo, zero_g, plan_s, plan_st, counted = (
            sem(s) for s in ("h_done", "silu", "hs", "z_done", "z_added", "loaded", "w_hi", "w_lo", "zero_g",
                             "plan_ready", "plan_stored", "counted"))
        xn_stored = [sem("xn_stored") for _ in range(2)]
        scattered = [sem("scattered") for _ in range(2)]
        held = sem("held")
        own_s, plan_own = sem("own"), sem("plan_own")
        R_STEPS = 15
        with nc.Block() as block:

            @block.sync
            def _(sp):
                sp.wait_ge(zero_g, 1)
                sp.dma_start(wg[:, :, 0:EXPERTS], a["wg"].rearrange("(c p) n -> p c n", p=P)).then_inc(loaded, 16)
                for s, n in ((w1, "ws1"), (w3, "ws3"), (w2, "ws2")):
                    sp.dma_start(s[:], a[n].rearrange("(c p) n -> p c n", p=P)).then_inc(loaded, 16)

                def body(m, u, g):
                    sp.wait_ge(xn_ready, m + 1)
                    sp.sem_inc(held, 1)
                    sp.dma_start(xn_rows[ds(m * MW, MW), :].rearrange("(t p) d -> p t d", p=P),
                                 XN[u][:]).then_inc(xn_stored[u], 16)
                every(sp, MACROS, body)
                for u in range(2):
                    sp.wait_ge(xn_stored[u], 16 * MACROS // 2)
                sp.wait_ge(plan_s, 1)
                for k in range(2):
                    with nc.allow_non_contiguous_dma("512 numbers"):
                        sp.dma_start(plan_rows[k].rearrange("(u p) -> p u", p=P), plan[:, :, k]).then_inc(plan_st, 16)
                sp.wait_ge(plan_st, 32)

            @block.gpsimd
            def _(pool):
                pool.memset(wg[:], 0.0).then_inc(zero_g, 1)
                pool.memset(counts[:], 0.0).then_inc(counted, 1)
                norm.power(pool, 0, 0)
                norm.power(pool, 1, 1)

                def body(m, u, g):
                    if not from_end(m, MACROS, 2):
                        norm.power(pool, m + 2, u)
                    pool.wait_ge(slots_s, m + 1)
                    pool.sem_inc(held, 1)
                    for t in range(MT):
                        for k in range(TOPK):
                            pool.indirect_dma_start(
                                token_of[:, :], bass.IndirectOffsetOnAxis(
                                    ap=slot_s[u][:, t * TOPK + k:t * TOPK + k + 1], axis=0),
                                tok_s[u][:, t:t + 1], None, bounds_check=SLOTS - 1, oob_is_err=False,
                            ).then_inc(scattered[u], 16)
                every(pool, MACROS, body)
                for u in range(2):
                    pool.wait_ge(scattered[u], 16 * MT * TOPK * MACROS // 2)

            @block.vector
            def _(dve):
                for n, s in (("wg", wg), ("w1", w1), ("w3", w3)):
                    dve.wait_ge(w_hi, 3)
                    dve.tensor_tensor(split[n][1][:], s[:], split[n][0][:], ALU.subtract).then_inc(w_lo, 1)
                own = Steps(dve, own_s, R_STEPS)
                norm.stats(dve, 0, 0)

                def gate(m, u, g):
                    dve.wait_ge(l_done, m + 1)
                    own.done(dve.tensor_reduce(mx[:], psL, X_AXIS, ALU.max))
                    dve.tensor_tensor(dl[:], psL, mx[:].unsqueeze(2).to_broadcast([P, MT, EXPERTS]),
                                      ALU.subtract).then_inc(l_shift, 1)
                    dve.wait_ge(l_exp, m + 1)
                    own.done(dve.tensor_reduce(sm[:], el[:], X_AXIS, ALU.add))
                    own.done(dve.reciprocal(rs[:], sm[:]))
                    own.done(dve.tensor_tensor(sc[:], el[:], rs[:].unsqueeze(2).to_broadcast([P, MT, EXPERTS]), ALU.mult))
                    dve.sem_inc(held, 1)
                    for t in range(MT):
                        last = dve.max(top[:, t, :], sc[:, t, :])
                    own.done(last)
                    dve.sem_inc(held, 1)
                    for t in range(MT):
                        last = dve.max_index(idx[:, t, :], top[:, t, :], sc[:, t, :])
                    own.done(last)
                    own.done(dve.tensor_copy(idf[:], idx[:, :, 0:TOPK]))
                    own.done(dve.tensor_tensor(
                        hot[:], idf[:].unsqueeze(3).to_broadcast([P, MT, TOPK, EXPERTS]),
                        expert_id[:].unsqueeze(1).unsqueeze(1).to_broadcast([P, MT, TOPK, EXPERTS]), ALU.is_equal))
                    with nc.allow_low_precision("zeros and ones"):
                        dve.tensor_reduce(chosen[:], hot[:].rearrange("p t k e -> p t e k"), X_AXIS,
                                          ALU.add).then_inc(chosen_s, 1)

                def place(m, u, g):
                    dve.wait_ge(c_done, m + 1)
                    if below(m, 1):
                        dve.wait_ge(counted, 1)
                    own.done(dve.tensor_tensor(pos[:], psC[:, 0:MT, :], counts[:].unsqueeze(1).to_broadcast(
                        [P, MT, EXPERTS]), ALU.add))
                    own.done(dve.tensor_tensor(counts[:], counts[:], psC[:, MT, :], ALU.add))
                    own.done(dve.tensor_scalar(pen[:], pos[:], float(CAP), float(4 * SLOTS), ALU.is_ge, ALU.mult))
                    own.done(dve.tensor_tensor(pos[:], pos[:], pen[:], ALU.add))
                    own.done(dve.scalar_tensor_tensor(
                        out=pos[:], in0=expert_id[:].unsqueeze(1).to_broadcast([P, MT, EXPERTS]), scalar=float(CAP),
                        in1=pos[:], op0=ALU.mult, op1=ALU.add))
                    own.done(dve.tensor_tensor(prod[:], hot[:], pos[:].unsqueeze(2).to_broadcast(
                        [P, MT, TOPK, EXPERTS]), ALU.mult))
                    own.done(dve.tensor_reduce(slotf[:], prod[:], X_AXIS, ALU.add))
                    if not below(m, 2):
                        dve.wait_ge(scattered[u], g * (16 * MT * TOPK))
                    flat = slotf[:].rearrange("p t k -> p (t k)")
                    dve.tensor_copy(slots[:, ds(m * (MT * TOPK), MT * TOPK)], flat)
                    dve.scalar_tensor_tensor(
                        out=gates[:, ds(m * (MT * TOPK), MT * TOPK)].rearrange("p (t k) -> p t k", k=TOPK),
                        in0=slotf[:], scalar=float(SLOTS) - 0.5, in1=top[:, :, 0:TOPK], op0=ALU.is_le, op1=ALU.mult)
                    dve.tensor_copy(tok_s[u][:], token_id[:, ds(m * MT, MT)])
                    dve.tensor_copy(slot_s[u][:], flat).then_inc(slots_s, 1)

                def hidden(m):
                    for o in range(KC):
                        dve.wait_ge(silu_s, m * KC + o + 1)
                        dve.wait_ge(h_done, m * 2 * KC + 2 * o + 2)
                        dve.tensor_tensor(HS[:, o], SG[:, o], psH[(2 * o + 1) % 3][:], ALU.mult).then_inc(hs_s, 1)

                def add_shared(m):
                    for h in range(2):
                        dve.wait_ge(z_done, m * 2 + h + 1)
                        dve.tensor_tensor(X[:, ds(m * MT + 2 * h, 2), :], X[:, ds(m * MT + 2 * h, 2), :],
                                          psZ[h], ALU.add).then_inc(z_added, 1)

                def low(m):
                    dve.wait_ge(x_hi, m + 1)
                    dve.tensor_tensor(XL[:], psX[:], XH[:], ALU.subtract).then_inc(x_lo, 1)
                norm.apply(dve, 0, 0, XN[0], xn_ready)
                norm.stats(dve, 1, 1)
                low(0)

                def body(m, u, g):
                    own.tile(m)
                    if not from_end(m, MACROS, 1):
                        if not below(m, 1):
                            dve.wait_ge(xn_stored[1 - u], (g if u == 0 else g + 1) * 16)
                        norm.apply(dve, m + 1, 1 - u, XN[1 - u], xn_ready)
                    if not from_end(m, MACROS, 2):
                        norm.stats(dve, m + 2, u)
                    gate(m, u, g)
                    hidden(m)
                    place(m, u, g)
                    if not from_end(m, MACROS, 1):
                        low(m + 1)
                    add_shared(m)
                every(dve, MACROS, body)

                own = Steps(dve, plan_own)
                own.done(dve.tensor_scalar(nt_i[0][:], counts[:], float(CAP), float(P - 1), ALU.min, ALU.add))
                own.done(dve.tensor_scalar(nt_i[1][:], nt_i[0][:], P.bit_length() - 1, None, ALU.arith_shift_right))
                dve.tensor_copy(ntile[:], nt_i[1][:])
                own.done(dve.tensor_copy(ends[0][:], nt_i[1][:]))
                s, k = 1, 0
                while s < EXPERTS:
                    dve.tensor_copy(ends[1 - k][:, 0:s], ends[k][:, 0:s])
                    own.done(dve.tensor_tensor(ends[1 - k][:, s:], ends[k][:, s:], ends[k][:, :EXPERTS - s], ALU.add))
                    s, k = 2 * s, 1 - k
                own.done(dve.tensor_tensor(shift[:], ends[k][:], ntile[:], ALU.subtract))
                own.done(dve.tensor_scalar(shift[:], shift[:], float(P), None, ALU.mult))
                own.done(dve.scalar_tensor_tensor(out=shift[:], in0=expert_id[:], scalar=-float(CAP), in1=shift[:],
                                                  op0=ALU.mult, op1=ALU.add))
                own.done(dve.tensor_tensor(le[:], ends[k][:].unsqueeze(1).to_broadcast([P, 2, EXPERTS]),
                                           tile_id[:].unsqueeze(2).to_broadcast([P, 2, EXPERTS]), ALU.is_le))
                own.done(dve.tensor_tensor(lew[:], le[:], ntile[:].unsqueeze(1).to_broadcast([P, 2, EXPERTS]), ALU.mult))
                dve.tensor_reduce(ej[:], le[:], X_AXIS, ALU.add)
                own.done(dve.tensor_reduce(sj[:], lew[:], X_AXIS, ALU.add))
                own.done(dve.tensor_tensor(sj[:], tile_id[:], sj[:], ALU.subtract))
                own.done(dve.tensor_scalar(aj[:], sj[:], float(P), None, ALU.mult))
                own.done(dve.scalar_tensor_tensor(out=aj[:], in0=ej[:], scalar=float(CAP), in1=aj[:],
                                                  op0=ALU.mult, op1=ALU.add))
                dve.tensor_scalar(plan[:, :, 0], ej[:], float(EXPERTS - 1), None, ALU.min)
                dve.tensor_scalar(plan[:, :, 1], aj[:], float(SLOTS + SPARE - P), None, ALU.min).then_inc(plan_s, 1)
                dve.wait_ge(slots_s, MACROS)
                pairs = [P, TILES * TOPK, EXPERTS]
                own.done(dve.tensor_scalar(e_i[:], slots[:], CAP.bit_length() - 1, None, ALU.arith_shift_right))
                own.done(dve.tensor_copy(e_f[:], e_i[:]))
                own.done(dve.tensor_tensor(pick[:], e_f[:].unsqueeze(2).to_broadcast(pairs),
                                           expert_id[:].unsqueeze(1).to_broadcast(pairs), ALU.is_equal))
                own.done(dve.tensor_tensor(pick[:], pick[:], shift[:].unsqueeze(1).to_broadcast(pairs), ALU.mult))
                own.done(dve.tensor_reduce(e_f[:], pick[:], X_AXIS, ALU.add))
                own.done(dve.tensor_tensor(slots[:], slots[:], e_f[:], ALU.add))

            @block.scalar
            def _(act):
                act.wait_ge(loaded, 64)
                for n, s in (("wg", wg), ("w1", w1), ("w3", w3)):
                    act.activation(split[n][0][:], s[:], ACT.Copy).then_inc(w_hi, 1)

                def high(m):
                    act.wait_ge(turned, m + 1)
                    if not below(m, 1):
                        act.wait_ge(h_done, m * 2 * KC)
                    act.activation(XH[:], psX[:], ACT.Copy).then_inc(x_hi, 1)
                high(0)

                def body(m, u, g):
                    act.wait_ge(g_done, m + 1)
                    act.activation(LT[0:EXPERTS, :], psG[0:EXPERTS, :], ACT.Copy).then_inc(g_out, 1)
                    act.wait_ge(l_shift, m + 1)
                    act.activation(el[:], dl[:], ACT.Exp).then_inc(l_exp, 1)
                    for o in range(KC):
                        act.wait_ge(h_done, m * 2 * KC + 2 * o + 1)
                        if not below(m, 1):
                            act.wait_ge(hs_s, m * KC)
                        act.activation(SG[:, o], psH[(2 * o) % 3][:], ACT.Silu).then_inc(silu_s, 1)
                    if not from_end(m, MACROS, 1):
                        high(m + 1)
                every(act, MACROS, body)

            @block.tensor
            def _(pe):
                pe.wait_ge(w_lo, 3)

                def product(dst, w, o):
                    terms = [(i, XX, c) for c in range(KC) for i, XX in ((0, XH), (0, XL), (1, XH))]
                    for n, (i, XX, c) in enumerate(terms):
                        last = pe.matmul(dst[:], split[w][i][:, c, o * P:(o + 1) * P], XX[:, c],
                                         start=n == 0, stop=n == len(terms) - 1)
                    return last

                def shared_out(m):
                    if not below(m, 1):
                        pe.wait_ge(z_added, m * 2 - 1)
                    pe.wait_ge(hs_s, m * KC + KC)
                    for t in range(MT):
                        for c in range(KC):
                            last = pe.matmul(psZ[t // 2][:, t % 2, :], HS[:, c, t * P:(t + 1) * P], w2[:, c, :],
                                             start=c == 0, stop=c == KC - 1)
                        if t % 2:
                            last.then_inc(z_done, 1)

                def turn_in(m, u):
                    pe.wait_ge(xn_ready, m + 1)
                    if not below(m, 1):
                        pe.wait_ge(x_lo, m)
                    turn(pe, XN[u], psX).then_inc(turned, 1)
                turn_in(0, 0)

                def body(m, u, g):
                    pe.wait_ge(x_lo, m + 1)
                    if not below(m, 1):
                        pe.wait_ge(z_added, m * 2)
                    terms = [(i, XX, c) for c in range(KC) for XX in (XH, XL) for i in (0, 1)]
                    for n, (i, XX, c) in enumerate(terms):
                        last = pe.matmul(psG[:], split["wg"][i][:, c, :], XX[:, c], start=n == 0,
                                         stop=n == len(terms) - 1)
                    last.then_inc(g_done, 1)
                    for o in range(KC):
                        for j, w in enumerate(("w1", "w3")):
                            b = (2 * o + j) % 3
                            if j == 0 and o == 0 and not below(m, 1):
                                pe.wait_ge(hs_s, m * KC)
                            if o == 1 and j == 0 and not below(m, 1):
                                pe.wait_ge(silu_s, m * KC)
                            if o == 1 and j == 1:
                                pe.wait_ge(silu_s, m * KC + 1)
                            product(psH[b], w, o).then_inc(h_done, 1)
                        if o == 0:
                            pe.wait_ge(g_out, m + 1)
                            if not below(m, 1):
                                pe.wait_ge(slots_s, m)
                            pe.sem_inc(held, 1)
                            for t in range(MT):
                                last = pe.transpose(psL[:, t, :], LT[0:EXPERTS, t * P:(t + 1) * P],
                                                    ident[0:EXPERTS, 0:EXPERTS])
                            last.then_inc(l_done, 1)
                    if not from_end(m, MACROS, 1):
                        turn_in(m + 1, 1 - u)
                    pe.wait_ge(chosen_s, m + 1)
                    for t in range(MT + 1):
                        for s in range(min(t + 1, MT)):
                            last = pe.matmul(psC[:, t, :], before[:] if s == t else ones_b[:], chosen[:, s, :],
                                             start=s == 0, stop=s == min(t, MT - 1))
                    last.then_inc(c_done, 1)
                    shared_out(m)
                every(pe, MACROS, body)
        st.close()

    def experts(W13, W2, w_loaded):
        st = ExitStack()
        ids = [space(st, "ids", [P, 1], I32) for _ in range(AHEAD)]
        XG = [space(st, "XG", [P, D]) for _ in range(AHEAD)]
        XT = [space(st, "XT", [P, KC, P]) for _ in range(2)]
        SG = [space(st, "SG", [P, HID]) for _ in range(2)]
        HB = [space(st, "HB", [P, HID]) for _ in range(2)]
        HT = [space(st, "HT", [P, P]) for _ in range(2)]
        YB = [space(st, "YB", [P, D]) for _ in range(AHEAD)]
        plan = space(st, "plan", [1, 2, 2 * P], I32)
        psX = [banks(st, "psX", [P, KC, P]) for _ in range(2)]
        psH = [banks(st, "psH", [P, 2 * HID]) for _ in range(2)]
        psT = [banks(st, "psT", [P, P]) for _ in range(2)]
        psY = [banks(st, "psY", [P, D]) for _ in range(2)]
        plan_in, turned, xt_out, h_done, silu_s, h_out, h_turned, ht_out, y_done, y_out, held = (sem(s) for s in (
            "plan_in", "turned", "xt_out", "h_done", "silu", "h_out", "h_turned", "ht_out", "y_done", "y_out", "held"))
        ids_in, gathered, stored = ([sem(s) for _ in range(AHEAD)] for s in ("ids_in", "gathered", "stored"))
        w13 = W13[:].rearrange("p e c n -> p (e c n)")
        w2 = W2[:].rearrange("p e n -> p (e n)")
        with nc.Block() as block:

            @block.sync
            def _(sp):
                sp.dma_start(plan[:], plan_rows.rearrange("(o k) j -> o k j", o=1)).then_inc(plan_in, 16)
                sp.wait_ge(plan_in, 16)

                def first_row(j):
                    return sp.value_load(plan[0:1, 1, ds(j, 1)], min_val=0, max_val=SLOTS + SPARE - P)

                def fetch(j, u, g):
                    row = first_row(j)
                    if g is not None:
                        sp.wait_ge(gathered[u], g * 16)
                        sp.sem_inc(held, 1)
                    sp.dma_start(ids[u][:], token_of[ds(row, P), :]).then_inc(ids_in[u], 16)

                def body(j, u, g):
                    sp.wait_ge(y_out, j + 1)
                    sp.sem_inc(held, 1)
                    sp.dma_start(y_rows[ds(j * P, P), :], YB[u][:]).then_inc(stored[u], 16)
                    if not from_end(j, ETILES, AHEAD):
                        fetch(j + AHEAD, u, g + 1)
                for u in range(AHEAD):
                    fetch(u, u, None)
                every(sp, ETILES, body, AHEAD)
                for u in range(AHEAD):
                    sp.wait_ge(stored[u], 16 * ETILES // AHEAD)

            @block.gpsimd
            def _(pool):
                def body(j, u, g):
                    pool.wait_ge(ids_in[u], g * 16 + 16)
                    pool.sem_inc(held, 1)
                    if not below(j, AHEAD):
                        pool.wait_ge(turned, j - AHEAD + 1)
                        pool.sem_inc(held, 1)
                    pool.indirect_dma_start(XG[u][:], None, xn_rows[:, :],
                                            bass.IndirectOffsetOnAxis(ap=ids[u][:, 0:1], axis=0)).then_inc(gathered[u], 16)
                every(pool, ETILES, body, AHEAD)

            @block.scalar
            def _(act):
                def turned_out(j, v):
                    act.wait_ge(turned, j + 1)
                    if not below(j, 2):
                        act.wait_ge(h_done, j - 1)
                    act.activation(XT[v][:], psX[v][:], ACT.Copy).then_inc(xt_out, 1)

                turned_out(0, 0)
                turned_out(1, 1)

                def body(j, u, g):
                    act.wait_ge(h_done, j + 1)
                    if not below(j, 2):
                        act.wait_ge(h_out, j - 1)
                    act.activation(SG[u % 2][:], psH[u % 2][:, 0:HID], ACT.Silu).then_inc(silu_s, 1)
                    if not from_end(j, ETILES, 2):
                        turned_out(j + 2, u % 2)
                every(act, ETILES, body, AHEAD)

            @block.vector
            def _(dve):
                def y_store(j, u, g):
                    dve.wait_ge(y_done, j + 1)
                    if g is not None:
                        dve.wait_ge(stored[u], g * 16)
                    dve.tensor_copy(YB[u][:], psY[u % 2][:]).then_inc(y_out, 1)

                def body(j, u, g):
                    if not below(j, 1):
                        v = (u + 1) % 2
                        dve.wait_ge(h_turned, j)
                        if not below(j, 3):
                            dve.wait_ge(y_done, j - 2)
                        dve.tensor_copy(HT[v][:], psT[v][:]).then_inc(ht_out, 1)
                    dve.wait_ge(silu_s, j + 1)
                    if not below(j, 2):
                        dve.wait_ge(h_turned, j - 1)
                    dve.tensor_tensor(HB[u % 2][:], SG[u % 2][:], psH[u % 2][:, HID:], ALU.mult).then_inc(h_out, 1)
                    if not below(j, 2):
                        y_store(j - 2, (u - 2) % AHEAD, None if below(j, AHEAD + 2) else (g if u >= 2 else g - 1))
                every(dve, ETILES, body, AHEAD)
                dve.wait_ge(h_turned, ETILES)
                dve.tensor_copy(HT[1][:], psT[1][:]).then_inc(ht_out, 1)
                for k in (2, 1):
                    y_store(ETILES - k, AHEAD - k, ETILES // AHEAD - 1)

            @block.tensor
            def _(pe):
                pe.wait_ge(plan_in, 16)
                pe.wait_ge(w_loaded[0], w_loaded[1])

                def turn_x(j, u, g):
                    pe.wait_ge(gathered[u], g * 16 + 16)
                    if not below(j, 2):
                        pe.wait_ge(xt_out, j - 1)
                    for c in range(KC):
                        last = pe.transpose(psX[u % 2][:, c], XG[u][:, c * P:(c + 1) * P], ident[:])
                    last.then_inc(turned, 1)

                regs = [pe.alloc_register(f"expert_{n}") for n in range(AHEAD)]
                before_regs = [pe.alloc_register(f"expert_before_{n}") for n in range(2)]

                def load_experts(j):
                    if not below(j, AHEAD):
                        pe.reg_mov(before_regs[0], regs[-2])
                        pe.reg_mov(before_regs[1], regs[-1])
                    pe.reg_load(regs, plan[0:1, 0, ds(j, AHEAD)])

                def expert(u):
                    return pe.snap(before_regs[u] if u < 0 else regs[u], min_val=0, max_val=EXPERTS - 1)

                def up(j, v, e):
                    pe.wait_ge(xt_out, j + 1)
                    if not below(j, 2):
                        pe.wait_ge(h_out, j - 1)
                    for c in range(KC):
                        last = pe.matmul(psH[v][:], XT[v][:, c], w13[:, ds(e * (KC * 2 * HID) + c * 2 * HID, 2 * HID)],
                                         start=c == 0, stop=c == KC - 1)
                    last.then_inc(h_done, 1)

                def turn_h(j, v):
                    pe.wait_ge(h_out, j + 1)
                    if not below(j, 2):
                        pe.wait_ge(ht_out, j - 1)
                    pe.transpose(psT[v][:], HB[v][:], ident[:]).then_inc(h_turned, 1)

                def down(j, v, e):
                    pe.wait_ge(ht_out, j + 1)
                    if not below(j, 2):
                        pe.wait_ge(y_out, j - 1)
                    pe.matmul(psY[v][:], HT[v][:], w2[:, ds(e * D, D)], start=True, stop=True).then_inc(y_done, 1)
                turn_x(0, 0, 0)
                turn_x(1, 1, 0)

                def body(j, u, g):
                    if u == 0:
                        load_experts(j)
                    up(j, u % 2, expert(u))
                    if not below(j, 1):
                        turn_h(j - 1, (u + 1) % 2)
                    if not below(j, 2):
                        down(j - 2, u % 2, expert(u - 2))
                    if not from_end(j, ETILES, 2):
                        turn_x(j + 2, (u + 2) % AHEAD, g + 1 if u >= AHEAD - 2 else g)
                every(pe, ETILES, body, AHEAD)
                turn_h(ETILES - 1, 1)
                down(ETILES - 2, 0, expert(AHEAD - 2))
                down(ETILES - 1, 1, expert(AHEAD - 1))
        st.close()

    class BinaryWeights:

        def __init__(self, st, W0, W1, W2, scale):
            self.out = (W0, W1, W2, scale)
            self.k0 = space(st, "k0", [P, 2 * KC, FEAT], U8)
            self.k1 = space(st, "k1", [P, FC, FEAT], U8)
            self.k2 = space(st, "k2", [P, FC, D], U8)
            self.k0f = space(st, "k0f", [P, KC, FEAT])
            self.s = space(st, "s", [P, 3])
            self.small = [space(st, n, [P, 3]) for n in ("negative", "positive", "sign", "twice", "size")]
            self.loaded, self.own_s = sem("binary_loaded"), sem("binary_own")

        def load(self, sp):
            for n in range(3):
                sp.dma_start(self.s[:, n:n + 1], a[f"s{n}"].rearrange("(o n) -> o n", o=1).to_broadcast(
                    [P, 1])).then_inc(self.loaded, 16)
            for k, n in ((self.k0, "k0"), (self.k1, "k1"), (self.k2, "k2")):
                sp.dma_start(k[:], a[n].rearrange("(c p) n -> p c n", p=P)).then_inc(self.loaded, 16)

        def prepare(self, dve):
            W0, W1, W2, scale = self.out
            neg, pos, sign, twice, size = self.small
            w = Steps(dve, self.own_s)
            dve.wait_ge(self.loaded, 96)
            dve.tensor_scalar(pos[:], self.s[:], 0.0, None, ALU.is_gt)
            w.done(dve.tensor_scalar(neg[:], self.s[:], 0.0, -1.0, ALU.is_lt, ALU.mult))
            w.done(dve.tensor_tensor(sign[:], pos[:], neg[:], ALU.add))
            w.done(dve.tensor_scalar(twice[:], sign[:], 2.0, None, ALU.mult))
            w.done(dve.tensor_tensor(size[:], self.s[:], twice[:], ALU.mult))
            w.done(dve.tensor_tensor(scale[:], size[:, 0:1], size[:, 1:2], ALU.mult))
            dve.tensor_tensor(scale[:], scale[:], self.s[:, 2:3], ALU.mult)
            w.done(dve.tensor_scalar(self.k0f[:], self.k0[:, 0:KC, :], twice[:, 0:1], None, ALU.mult))
            w.done(dve.tensor_scalar(W0[:], self.k0[:, KC:, :], twice[:, 0:1], None, ALU.mult))
            dve.tensor_tensor(W0[:], self.k0f[:], W0[:], ALU.subtract)
            dve.tensor_scalar(W1[:], self.k1[:], twice[:, 1:2], sign[:, 1:2], ALU.mult, ALU.subtract)
            dve.tensor_scalar(W2[:], self.k2[:], 2.0, -1.0, ALU.mult, ALU.add)

    class Combine:

        def __init__(self, st):
            self.G = [space(st, "G", [P, TOPK, D]) for _ in range(MT)]
            self.SI = [space(st, "SI", [P, MT * TOPK], I32) for _ in range(2)]
            self.cleared, self.staged, self.summed, self.own_s, self.held = (
                sem(n) for n in ("g_cleared", "g_staged", "summed", "sum_own", "g_held"))
            self.gathered = [sem("gathered") for _ in range(MT)]

        def clear(self, pool):
            for g in self.G:
                pool.memset(g[:], 0.0).then_inc(self.cleared, 1)
            pool.wait_ge(self.cleared, MT)

        def gather(self, pool, m, u):
            if not below(m, 2):
                pool.wait_ge(self.summed, m * MT - MT)
            pool.tensor_copy(self.SI[u][:], slots[:, ds(m * (MT * TOPK), MT * TOPK)]).then_inc(self.staged, 1)
            pool.wait_ge(self.staged, m + 1)
            pool.sem_inc(self.held, 1)
            for t in range(MT):
                if not below(m, 1):
                    pool.wait_ge(self.summed, m * MT - MT + t + 1)
                    pool.sem_inc(self.held, 1)
                for k in range(TOPK):
                    pool.indirect_dma_start(
                        self.G[t][:, k, :], None, y_rows[:, :], bass.IndirectOffsetOnAxis(
                            ap=self.SI[u][:, t * TOPK + k:t * TOPK + k + 1], axis=0),
                        bounds_check=ETILES * P - 1, oob_is_err=False).then_inc(self.gathered[t], 16)

        def add(self, dve, m):
            own = Steps(dve, self.own_s, MT * TOPK)
            own.tile(m)
            for t in range(MT):
                dve.wait_ge(self.gathered[t], m * (16 * TOPK) + 16 * TOPK)
                for k in range(TOPK):
                    own.done(dve.scalar_tensor_tensor(
                        out=X[:, ds(m * MT + t, 1), :], in0=self.G[t][:, k:k + 1, :],
                        scalar=gates[:, ds((m * MT + t) * TOPK + k, 1)], in1=X[:, ds(m * MT + t, 1), :],
                        op0=ALU.mult, op1=ALU.add))
                dve.sem_inc(self.summed, 1)

    def ffn(W0, W1, W2, scale):
        st = ExitStack()
        XN = space(st, "XN", [P, MT, D])
        XH, XL = (space(st, n, [P, KC, MW], F32R) for n in ("XH", "XL"))
        H = [[space(st, "H", [P, FC, MW], F32R) for _ in range(2)] for _ in range(2)]
        OT = space(st, "OT", [P, KC, MW])
        OUT = [space(st, "OUT", [P, MT, D]) for _ in range(2)]
        norm = Norm(st)
        psX = banks(st, "psX", [P, KC, MW])
        psA = [banks(st, "psA", [P, MW]) for _ in range(4)]
        psB = banks(st, "psB", [P, MT, D])
        xn_ready, turned, x_hi, x_lo, done, hi, lo, back, final = (sem(n) for n in (
            "xn_ready", "turned", "x_hi", "x_lo", "product_done", "high_out", "low_out", "turned_back", "final"))
        stored = [sem("stored") for _ in range(2)]
        G = 2 * FC + KC
        with nc.Block() as block:

            @block.gpsimd
            def _(pool):
                every(pool, MACROS, lambda m, u, g: norm.power(pool, m, u))

            @block.vector
            def _(dve):
                def split_low(m):
                    dve.wait_ge(x_hi, m + 1)
                    dve.tensor_tensor(XL[:], psX[:], XH[:], ALU.subtract).then_inc(x_lo, 1)

                def relu_low(m, layer):
                    for o in range(FC):
                        k = layer * FC + o
                        dve.wait_ge(hi, m * G + k + 1)
                        dve.scalar_tensor_tensor(out=H[layer][1][:, o], in0=psA[k % 4][:], scalar=0.0,
                                                 in1=H[layer][0][:, o], op0=ALU.max, op1=ALU.subtract).then_inc(lo, 1)

                def finish(m, u, g):
                    dve.wait_ge(back, m + 1)
                    if g is not None:
                        dve.wait_ge(stored[u], g * 16)
                    dve.scalar_tensor_tensor(out=OUT[u][:], in0=psB[:], scalar=scale[:, 0:1],
                                             in1=X[:, ds(m * MT, MT), :], op0=ALU.mult, op1=ALU.add).then_inc(final, 1)
                norm.stats(dve, 0, 0)
                norm.apply(dve, 0, 0, XN, xn_ready)
                norm.stats(dve, 1, 1)
                split_low(0)

                def body(m, u, g):
                    last = isinstance(m, int) and m == MACROS - 1
                    if not last:
                        dve.wait_ge(turned, m + 1)
                        norm.apply(dve, m + 1, 1 - u, XN, xn_ready)
                    if not from_end(m, MACROS, 2):
                        norm.stats(dve, m + 2, u)
                    relu_low(m, 0)
                    if not below(m, 1):
                        finish(m - 1, 1 - u, None if below(m, 3) else (g if u else g - 1))
                    if not last:
                        split_low(m + 1)
                    relu_low(m, 1)
                every(dve, MACROS, body)
                finish(MACROS - 1, 1, MACROS // 2 - 1)

            @block.scalar
            def _(act):
                def split_high(m):
                    act.wait_ge(turned, m + 1)
                    act.activation(XH[:], psX[:], ACT.Copy).then_inc(x_hi, 1)

                def relu_high(m, layer):
                    for o in range(FC):
                        k = layer * FC + o
                        act.wait_ge(done, m * G + k + 1)
                        act.activation(H[layer][0][:, o], psA[k % 4][:], ACT.Relu).then_inc(hi, 1)
                split_high(0)

                def body(m, u, g):
                    relu_high(m, 0)
                    if not (isinstance(m, int) and m == MACROS - 1):
                        split_high(m + 1)
                    relu_high(m, 1)
                    for o in range(KC):
                        act.wait_ge(done, m * G + 2 * FC + o + 1)
                        if not below(m, 1):
                            act.wait_ge(back, m)
                        act.activation(OT[:, o], psA[(2 * FC + o) % 4][:], ACT.Copy).then_inc(hi, 1)
                every(act, MACROS, body)

            @block.tensor
            def _(pe):
                def free(m, k):
                    if k >= 4:
                        pm, pk = m, k - 4
                    elif below(m, 1):
                        return
                    else:
                        pm, pk = m - 1, (2 * FC + k if k < KC else 2 * FC - 4 + k)
                    pe.wait_ge(hi, pm * G + pk + 1)
                    if pk < 2 * FC:
                        pe.wait_ge(lo, pm * (2 * FC) + pk + 1)

                def layer(m, k0, W, cols, src, n_in, ready):
                    for o in range(cols):
                        free(m, k0 + o)
                        n = 0
                        for c in range(n_in):
                            if o == 0:
                                ready(c)
                            for part in range(2):
                                last = pe.matmul(psA[(k0 + o) % 4][:], W[:, c, o * P:(o + 1) * P], src[part][:, c],
                                                 start=n == 0, stop=n == 2 * n_in - 1)
                                n += 1
                        last.then_inc(done, 1)

                def turn_in(m):
                    pe.wait_ge(xn_ready, m + 1)
                    if not below(m, 1):
                        pe.wait_ge(x_lo, m)
                    turn(pe, XN, psX).then_inc(turned, 1)

                def turn_out(m):
                    pe.wait_ge(hi, m * G + G)
                    if not below(m, 1):
                        pe.wait_ge(final, m)
                    for t in range(MT):
                        for c in range(KC):
                            last = pe.transpose(psB[:, t, c * P:(c + 1) * P], OT[:, c, t * P:(t + 1) * P], ident[:])
                    last.then_inc(back, 1)
                turn_in(0)

                def body(m, u, g):
                    layer(m, 0, W0, FC, (XH, XL), KC, lambda c: pe.wait_ge(x_lo, m + 1))
                    if not below(m, 1):
                        turn_out(m - 1)
                    if not (isinstance(m, int) and m == MACROS - 1):
                        turn_in(m + 1)
                    layer(m, FC, W1, FC, H[0], FC, lambda c: pe.wait_ge(lo, m * (2 * FC) + c + 1))
                    layer(m, 2 * FC, W2, KC, H[1], FC, lambda c: pe.wait_ge(lo, m * (2 * FC) + FC + c + 1))
                every(pe, MACROS, body)
                turn_out(MACROS - 1)

            @block.sync
            def _(sp):
                def body(m, u, g):
                    sp.wait_ge(final, m + 1)
                    sp.sem_inc(norm.held, 1)
                    sp.dma_start(out_rows[ds(m * MW, MW), :].rearrange("(t p) d -> p t d", p=P),
                                 OUT[u][:]).then_inc(stored[u], 16)
                every(sp, MACROS, body)
                for u in range(2):
                    sp.wait_ge(stored[u], 16 * MACROS // 2)
        st.close()

    out_rows = out.rearrange("b s d -> (b s) d")

    def attention(w, masked, after_experts, binary_out):
        st = ExitStack()
        QT = space(st, "QT", [P, KC, TOKENS])
        KB = space(st, "KB", [P, BATCH, KC, HH, KEYS])
        V1, V2, V3 = (space(st, "V", [P, BATCH, PCH, 3 * VW], BF16) for _ in range(3))
        keys_values(w, KB, V1, V2, V3, binary_out)
        queries(w, QT, after_experts)
        attend(w, QT, KB, V1, V2, V3, masked)
        st.close()
        retire()

    with whole:
        setup()
        attention({k: a[f"l0_{k}"] for k in ("wq", "bq", "wk", "bk", "wv", "bv", "wo", "bo")}, True, False, None)
        moe = ExitStack()
        W13 = space(moe, "W13", [P, EXPERTS, KC, 2 * HID])
        W2 = space(moe, "W2", [P, EXPERTS, D])
        counts = space(moe, "counts", [P, EXPERTS])
        shift = space(moe, "shift", [P, EXPERTS])
        w_loaded = sem("w_loaded")
        with nc.Block() as block:

            @block.sync
            def _(sp):
                for c in range(KC):
                    for j, n in enumerate(("w1", "w3")):
                        sp.dma_start(W13[:, :, c, j * HID:(j + 1) * HID],
                                     a[n][:, c * P:(c + 1) * P, :].rearrange("e p h -> p e h")).then_inc(w_loaded, 16)
                sp.dma_start(W2[:], a["w2"].rearrange("e h d -> h e d")).then_inc(w_loaded, 16)
        route(counts, shift)
        experts(W13, W2, (w_loaded, 16 * (2 * KC + 1)))
        moe.close()
        last = ExitStack()
        B0 = space(last, "B0", [P, KC, FEAT], F32R)
        B1 = space(last, "B1", [P, FC, FEAT], F32R)
        B2 = space(last, "B2", [P, FC, D], F32R)
        scale = space(last, "scale", [P, 1])
        attention({k: a[f"l1_{k}"] for k in ("wq", "bq", "wk", "bk", "wv", "bv", "wo", "bo")}, False, True,
                  (B0, B1, B2, scale))
        ffn(B0, B1, B2, scale)
        last.close()


_INS = {
    "x": "x", "ctx": "ctx_1024", "mask": "mask_SxS2_bk1",
    "l0_wq": "L0_xattn_W_q", "l0_bq": "L0_xattn_b_q", "l0_wk": "L0_xattn_W_k", "l0_bk": "L0_xattn_b_k",
    "l0_wv": "L0_xattn_W_v", "l0_bv": "L0_xattn_b_v", "l0_wo": "L0_xattn_W_o", "l0_bo": "L0_xattn_b_o",
    "wg": "L0_ffn_Wg", "w1": "L0_ffn_W1", "w2": "L0_ffn_W2", "w3": "L0_ffn_W3",
    "ws1": "L0_ffn_Ws1", "ws2": "L0_ffn_Ws2", "ws3": "L0_ffn_Ws3",
    "l1_wq": "L1_xattn_Wq", "l1_bq": "L1_xattn_bq", "l1_wk": "L1_xattn_Wk", "l1_bk": "L1_xattn_bk",
    "l1_wv": "L1_xattn_Wv", "l1_bv": "L1_xattn_bv", "l1_wo": "L1_xattn_We", "l1_bo": "L1_xattn_be",
    "k0": "L1_ffn_k0", "k1": "L1_ffn_k1", "k2": "L1_ffn_k2",
    "s0": "L1_ffn_s0", "s1": "L1_ffn_s1", "s2": "L1_ffn_s2",
}


def kernel(**inputs):
    import numpy as _np
    import concourse.bacc as _bacc
    from concourse import mybir as _mybir
    from concourse.bass_utils import run_bass_kernel_spmd as _run

    nc = _bacc.Bacc("TRN2", target_bir_lowering=False, num_devices=1)
    arrays, aps = {}, {}
    for short, name in _INS.items():
        v = _np.ascontiguousarray(inputs[name])
        if v.ndim == 0:
            v = v.reshape(1)
        arrays[f"in_{short}"] = v
        aps[short] = nc.dram_tensor(f"in_{short}", v.shape, _mybir.dt.from_np(v.dtype), kind="ExternalInput").ap()
    out = nc.dram_tensor("out_x", (BATCH, SEQ, D), F32, kind="ExternalOutput").ap()
    build(nc, aps, out)
    r = _run(nc, [arrays], core_ids=[0])
    return r.results[0]["out_x"]
```
